# Optimizing a Trainium2 kernel written in Bass

```python
import numpy as np
import jax
import jax.numpy as jnp

def _softmax(x, axis=-1):
    return jax.nn.softmax(x, axis=axis)

def _gelu(x):
    return jax.nn.gelu(x, approximate=True)

def _silu(x):
    return jax.nn.silu(x)

def _sigmoid(x):
    return jax.nn.sigmoid(x)

def _layernorm(x, axis=-1, eps=1e-05):
    m = jnp.mean(x, axis=axis, keepdims=True)
    v = jnp.var(x, axis=axis, keepdims=True)
    return (x - m) / jnp.sqrt(v + eps)

def _scatter_add(tgt, idx, src, axis=0):
    return tgt.at[idx].add(src)

def _segment_sum(src, seg, n):
    return jax.ops.segment_sum(src, seg, n)
kernel_name = 'mk_gnn_ffn_d1_gnn_r32_0327f9'

def setup_inputs(seed: int=0):
    np.random.seed(seed)
    _w = jnp.asarray

    def _rec_inputs():
        import jax
        import jax.numpy as jnp
        _gk = jax.random.key(seed)
        x = -0.0002117 + 1 * jax.random.normal(jax.random.fold_in(_gk, 1), (3125, 256), jnp.float32)
        _s = jax.random.randint(jax.random.fold_in(_gk, 2), (25000,), 0, 3125, jnp.int32)
        _d = jax.random.randint(jax.random.fold_in(_gk, 3), (25000,), 0, 3125, jnp.int32)
        _loop = jnp.arange(3125, dtype=jnp.int32)
        src = jnp.concatenate([_s, _d, _loop])
        dst = jnp.concatenate([_d, _s, _loop])
        _o = jnp.argsort(dst, stable=True)
        src = src[_o]
        dst = dst[_o]
        return (x, src, dst)
    x, src, dst = _rec_inputs()

    def _L0_gnn_setup():
        import jax, jax.numpy as jnp
        import numpy as np
        N = 3125
        D = 256
        E = 9375
        BN_EPS = 1e-05

        def _batchnorm(x, gamma, beta):
            mean = jnp.mean(x, axis=0)
            var = jnp.var(x, axis=0)
            return (x - mean) * jax.lax.rsqrt(var + BN_EPS) * gamma + beta
        key = jax.random.key(seed)
        ks = jax.random.split(key, 8)
        h = jax.random.normal(ks[0], (N, D), dtype=jnp.float32)
        edge_index = jax.random.randint(ks[1], (2, E), 0, N, dtype=jnp.int64)
        W1 = jax.random.normal(ks[2], (D, 2 * D), dtype=jnp.float32) / np.sqrt(D)
        b1 = jnp.zeros((2 * D,), dtype=jnp.float32)
        g1 = jnp.ones((2 * D,), dtype=jnp.float32)
        bt1 = jnp.zeros((2 * D,), dtype=jnp.float32)
        W2 = jax.random.normal(ks[3], (2 * D, D), dtype=jnp.float32) / np.sqrt(2 * D)
        b2 = jnp.zeros((D,), dtype=jnp.float32)
        g2 = jnp.ones((D,), dtype=jnp.float32)
        bt2 = jnp.zeros((D,), dtype=jnp.float32)
        eps_gin = jnp.zeros((), dtype=jnp.float32)
        return {'h': h, 'edge_index': edge_index, 'W1': W1, 'b1': b1, 'g1': g1, 'bt1': bt1, 'W2': W2, 'b2': b2, 'g2': g2, 'bt2': bt2, 'eps_gin': eps_gin}
    _L0_gnn_all = _L0_gnn_setup()
    _L0_gnn_in = {k: v for k, v in _L0_gnn_all.items() if k in ('W1', 'b1', 'g1', 'bt1', 'W2', 'b2', 'g2', 'bt2', 'eps_gin')}
    del _L0_gnn_all

    def _L0_ffn_setup():
        import jax, jax.numpy as jnp
        import numpy as np
        TOP_K = 2
        LN_EPS = 1e-05
        key = jax.random.key(seed)
        ks = jax.random.split(key, 8)
        B, S, D, E, H = (16, 1024, 256, 8, 1024)
        x = jax.random.normal(ks[0], (B, S, D), dtype=jnp.float32)
        Wr = jax.random.normal(ks[1], (D, E), dtype=jnp.float32) * 0.1
        br = jnp.zeros((E,), dtype=jnp.float32)
        ln_g = jnp.ones((E, D), dtype=jnp.float32)
        ln_b = jnp.zeros((E, D), dtype=jnp.float32)
        W1 = jax.random.normal(ks[2], (E, D, H), dtype=jnp.float32) * (1.0 / np.sqrt(D))
        b1 = jnp.zeros((E, H), dtype=jnp.float32)
        W2 = jax.random.normal(ks[3], (E, H, D), dtype=jnp.float32) * (1.0 / np.sqrt(H))
        b2 = jnp.zeros((E, D), dtype=jnp.float32)
        return {'x': x, 'Wr': Wr, 'br': br, 'ln_g': ln_g, 'ln_b': ln_b, 'W1': W1, 'b1': b1, 'W2': W2, 'b2': b2}
    _L0_ffn_all = _L0_ffn_setup()
    _L0_ffn_in = {k: v for k, v in _L0_ffn_all.items() if k in ('Wr', 'br', 'ln_g', 'ln_b', 'W1', 'b1', 'W2', 'b2')}
    del _L0_ffn_all
    return {'x': x, 'src': src, 'dst': dst, 'L0_gnn_W1': _L0_gnn_in['W1'], 'L0_gnn_b1': _L0_gnn_in['b1'], 'L0_gnn_g1': _L0_gnn_in['g1'], 'L0_gnn_bt1': _L0_gnn_in['bt1'], 'L0_gnn_W2': _L0_gnn_in['W2'], 'L0_gnn_b2': _L0_gnn_in['b2'], 'L0_gnn_g2': _L0_gnn_in['g2'], 'L0_gnn_bt2': _L0_gnn_in['bt2'], 'L0_gnn_eps_gin': _L0_gnn_in['eps_gin'], 'L0_ffn_Wr': _L0_ffn_in['Wr'], 'L0_ffn_br': _L0_ffn_in['br'], 'L0_ffn_ln_g': _L0_ffn_in['ln_g'], 'L0_ffn_ln_b': _L0_ffn_in['ln_b'], 'L0_ffn_W1': _L0_ffn_in['W1'], 'L0_ffn_b1': _L0_ffn_in['b1'], 'L0_ffn_W2': _L0_ffn_in['W2'], 'L0_ffn_b2': _L0_ffn_in['b2']}

def reference(x, src, dst, L0_gnn_W1, L0_gnn_b1, L0_gnn_g1, L0_gnn_bt1, L0_gnn_W2, L0_gnn_b2, L0_gnn_g2, L0_gnn_bt2, L0_gnn_eps_gin, L0_ffn_Wr, L0_ffn_br, L0_ffn_ln_g, L0_ffn_ln_b, L0_ffn_W1, L0_ffn_b1, L0_ffn_W2, L0_ffn_b2):
    import jax
    import jax.numpy as jnp

    def _L0_gnn_ref(h, edge_index, W1, b1, g1, bt1, W2, b2, g2, bt2, eps_gin):
        import jax, jax.numpy as jnp
        import numpy as np
        N = 3125
        D = 256
        E = 9375
        BN_EPS = 1e-05

        def _batchnorm(x, gamma, beta):
            mean = jnp.mean(x, axis=0)
            var = jnp.var(x, axis=0)
            return (x - mean) * jax.lax.rsqrt(var + BN_EPS) * gamma + beta
        src, dst = (edge_index[0], edge_index[1])
        agg = jax.ops.segment_sum(h[src], dst, num_segments=N)
        z = (1.0 + eps_gin) * h + agg
        t = jnp.dot(z, W1) + b1
        t = jax.nn.relu(_batchnorm(t, g1, bt1))
        conv_out = jnp.dot(t, W2) + b2
        out = jax.nn.relu(_batchnorm(conv_out + h, g2, bt2))
        return out

    def _L0_ffn_ref(x, Wr, br, ln_g, ln_b, W1, b1, W2, b2):
        import jax, jax.numpy as jnp
        import numpy as np
        TOP_K = 2
        LN_EPS = 1e-05
        B, S, D = x.shape
        N = B * S
        xt = x.reshape(N, D)
        logits = xt @ Wr + br
        probs = jax.nn.softmax(logits, axis=-1)
        top_p, top_idx = jax.lax.top_k(probs, TOP_K)
        weights = top_p / top_p.sum(axis=-1, keepdims=True)
        mu = xt.mean(axis=-1, keepdims=True)
        var = ((xt - mu) ** 2).mean(axis=-1, keepdims=True)
        xn = (xt - mu) * jax.lax.rsqrt(var + LN_EPS)
        xe = xn[None, :, :] * ln_g[:, None, :] + ln_b[:, None, :]
        h = jax.nn.gelu(jnp.einsum('end,edh->enh', xe, W1) + b1[:, None, :], approximate=False)
        y = jnp.einsum('enh,ehd->end', h, W2) + b2[:, None, :]
        y_tok = jnp.transpose(y, (1, 0, 2))
        sel = jnp.take_along_axis(y_tok, top_idx[:, :, None], axis=1)
        out = (weights[:, :, None] * sel).sum(axis=1)
        return out.reshape(B, S, D)
    edge_index = jnp.stack([src, dst])
    x = x + _L0_gnn_ref(_layernorm(x, axis=-1), edge_index, L0_gnn_W1, L0_gnn_b1, L0_gnn_g1, L0_gnn_bt1, L0_gnn_W2, L0_gnn_b2, L0_gnn_g2, L0_gnn_bt2, L0_gnn_eps_gin)
    x = x + _L0_ffn_ref(_layernorm(x, axis=-1)[None], L0_ffn_Wr, L0_ffn_br, L0_ffn_ln_g, L0_ffn_ln_b, L0_ffn_W1, L0_ffn_b1, L0_ffn_W2, L0_ffn_b2)[0]
    return x

_drawn_inputs = setup_inputs


def setup_inputs(seed=0):
    import zlib

    import numpy as np

    out = dict(_drawn_inputs(seed))
    spreads = {'L0_gnn_b1': (0.0, 0.1),
     'L0_gnn_g1': (1.0, 0.2),
     'L0_gnn_bt1': (0.0, 0.1),
     'L0_gnn_b2': (0.0, 0.1),
     'L0_gnn_g2': (1.0, 0.2),
     'L0_gnn_bt2': (0.0, 0.1),
     'L0_ffn_br': (0.0, 0.1),
     'L0_ffn_ln_g': (1.0, 0.2),
     'L0_ffn_ln_b': (0.0, 0.1),
     'L0_ffn_b1': (0.0, 0.1),
     'L0_ffn_b2': (0.0, 0.1)}
    factors = {}
    for name, (base, spread) in spreads.items():
        noise = np.random.default_rng([zlib.crc32(name.encode()), seed]).standard_normal(out[name].shape)
        drawn = base * np.exp(spread * noise) if base else spread * noise
        out[name] = jnp.asarray(drawn.astype(out[name].dtype))
    for name, factor in factors.items():
        out[name] = (out[name] * factor).astype(out[name].dtype)
    return out
```

```python
from contextlib import ExitStack

import numpy as np
import concourse.bass as bass
from concourse import mybir

F32 = mybir.dt.float32
F16 = mybir.dt.float16
I32 = mybir.dt.int32
U32 = mybir.dt.uint32
ALU = mybir.AluOpType
ACT = mybir.ActivationFunctionType
AX = mybir.AxisListType

N, D, E = 3125, 256, 53125
P = 125
C = N // P
G, S = 5, 5
XG = 4
HID = 2 * D
X, H = 8, 1024
EPS = 1e-5
BW, BJ = 16, 8
NB = C * BJ
HB = NB // 2
U = 3
WIN = U * P
PITCH = 25
NWIN = (E - WIN) // PITCH + 1
EROW = E // P
SEG = EROW // PITCH
KEY = BW * C
WSCALE = 64.0
MAGIC = 12582912.0
PIECES = [(500 * i, min(500, N - 500 * i)) for i in range(7)]
T = 128
CAP = -(-(N + T) // T) * T
NT = -(-2 * N // T) + X
TAB = NT + 3
SPARE = TAB - (-(-2 * N // T))
ROW = D + 1
V_B1, V_LNG, V_LNB = 0, X * 8, X * 8 + 2 * X
V_GB1 = V_LNB + 2 * X
V_GG1, V_GBT1, V_GB2, V_GG2, V_GBT2 = V_GB1 + 4, V_GB1 + 8, V_GB1 + 12, V_GB1 + 14, V_GB1 + 16
NV = V_GB1 + 18
PARTS = 4 * X
EARLY, AFTER_SUM, AFTER_CONV = 8, 10, 20


def width(j):
    return min(BW, P - BW * j)


class Steps:

    def __init__(self, sem):
        self.sem, self.n = sem, 0

    def inc(self, ins):
        ins.then_inc(self.sem, 1)
        self.n += 1
        return self.n


def build(nc, x, src, dst, gW1, gb1, gg1, gbt1, gW2, gb2, gg2, gbt2, eps_gin, Wr, br, ln_g, ln_b,
          W1, b1, W2, b2, out):
    ctx = ExitStack()
    with ctx:
        base = (nc.sbuf_base + 31) // 32 * 32
        top = nc.sbuf_usable_end - 128
        ctx.enter_context(nc.sbuf_tensor("arena", [128, top - base], mybir.dt.uint8))
        at = {"now": base}

        def place(name, shape, dt, offset=None):
            size = int(np.prod(shape[1:])) * mybir.dt.size(dt)
            if offset is None:
                offset = at["now"]
                at["now"] = offset + (size + 31) // 32 * 32
            assert offset + size <= top, (name, offset + size - top)
            return nc.alloc_sbuf_tensor_at(name, shape, dt, offset=offset)

        def sem(name):
            return ctx.enter_context(nc.semaphore(name))

        bank = [ctx.enter_context(nc.psum_tensor(f"bank{i}", [128, 512], F32)) for i in range(8)]

        ident = place("ident", [128, 128], F32)
        key_iota = place("key_iota", [P, KEY], F16)
        before16 = place("before16", [P, P], F16)
        ones16 = place("ones16", [128, 128], F16)
        ones = place("ones", [128, 128], F32)
        node0 = place("node0", [P, (C + 1) * BJ], F32)
        expert_iota = place("expert_iota", [P, X], F32)
        expert_row = place("expert_row", [P, X], F32)
        token_id = place("token_id", [P, 2, C], I32)
        tile_no = place("tile_no", [X, TAB], F32)
        upto = place("upto", [X, X], F32)
        vrows = place("vrows", [NV, 128], F32)
        vcols = place("vcols", [128, NV], F32)
        eps1 = place("eps1", [P, 1], F32)
        Wr_sb = place("Wr_sb", [128, 2, X], F32)
        br_sb = place("br_sb", [1, X], F32)
        x2 = place("x2", [P, C, D], F32)
        h32 = x2
        bn1 = place("bn1", [128, 4, 7, 6], F32)
        bn2 = place("bn2", [128, 2, 7, 6], F32)
        bn_mv = place("bn_mv", [128, 6, 2], F32)
        bn_var = place("bn_var", [128, 6], F32)
        bn_std = place("bn_std", [128, 6], F32)
        bn_r = place("bn_r", [128, 6], F32)
        bn_scale = place("bn_scale", [128, 6], F32)
        bn_ms = place("bn_ms", [128, 6], F32)
        bn_shift = place("bn_shift", [128, 6], F32)
        kc = [place(f"kc{i}", [P, 2, BJ, U], F32) for i in range(2)]
        flag = place("flag", [1, 1], I32)
        cnt = place("cnt", [HB, 6], F32)
        startf = place("startf", [HB, 2], F32)
        starti = place("starti", [HB, 2], I32)
        missed = place("missed", [HB, 2], F32)
        bad = place("bad", [P, 2], F32)
        next_dst = place("next_dst", [P, 1], I32)
        stats = [place(f"stats{i}", [P, S, 6], F32) for i in range(2)]
        mv = [place(f"mv{i}", [P, S, 2], F32) for i in range(2)]
        var_eps = [place(f"var_eps{i}", [P, S], F32) for i in range(2)]
        std = [place(f"std{i}", [P, S], F32) for i in range(2)]
        rstd = [place(f"rstd{i}", [P, S], F32) for i in range(2)]
        shift = [place(f"shift{i}", [P, S], F32) for i in range(2)]
        logits = place("logits", [P, S, X], F32)
        best = place("best", [P, S, X], F32)
        best_at = place("best_at", [P, S, X], U32)
        pick = place("pick", [P, 2, S], F32)
        hot = place("hot", [P, 2, S, X], F16)
        both = place("both", [P, S, X], F16)
        group_sum = place("group_sum", [P, X], F32)
        chosen = place("chosen", [P, X], F16)
        slot = place("slot", [P, S, X], F32)
        picked = place("picked", [P, 2, S, X], F32)
        slotf = place("slotf", [P, 2, S], F32)
        sloti = place("sloti", [P, 2, S], I32)
        gap = place("gap", [P, C], F32)
        gap_exp = place("gap_exp", [P, C], F32)
        gap_sum = place("gap_sum", [P, C], F32)
        mix = place("mix", [P, 2, C], F32)
        steps = place("steps", [X, 8], F32)
        passed = place("passed", [X, 2, TAB], F32)
        tile_row = place("tile_row", [1, TAB], I32)
        tile_expert = place("tile_expert", [1, TAB], I32)
        pad_at = place("pad_at", [1, X], I32)
        wait_src = place("wait_src", [1, 8], F32)
        after_wait = place("after_wait", [1, 8], F32)
        pad_row = place("pad_row", [128, ROW], F32)
        b2_all = place("b2_all", [128, X, D], F32)
        stage = [place(f"stage{i}", [128, 1024], F32) for i in range(3)]
        wbase = at["now"]
        wts = place("wts", [128, X * 4 * 2048], F16)
        WSZ = 4 * 2048 * 2
        work = at["now"]
        o = wbase + 2 * WSZ
        h16 = place("h16", [P, C, 2 * D], F16, o)
        o += C * 2 * D * 2
        counts = [place(f"counts{i}", [P, C, P], F16, o + i * 6272) for i in range(2)]
        xraw = place("xraw", [P, C, D], F32, o)
        agg = place("agg", [P, C, D], F32, o)
        o_fb = o + C * D * 4
        o += 2 * 6272
        key_hot = place("key_hot", [P, BJ, U, KEY], F16, o)
        o += BJ * U * KEY * 2
        low_hot = place("low_hot", [P, BJ, U, P], F16, o)
        o += BJ * U * P * 2 + 16
        keys = place("keys", [P, NB, U], F32, o)
        lows = place("lows", [P, NB, U], F32, o + NB * U * 4)
        o += 2 * NB * U * 4
        gathered = place("gathered", [P, D], F32, o_fb)
        fb_hot = place("fb_hot", [P, P], F32, o_fb + 1024)
        src_nat = place("src_nat", [P, EROW], I32, o_fb + 1536)
        fb_index = place("fb_index", [P, 1], I32, o_fb + 3264)
        fb_dst = place("fb_dst", [P, 1], F32, o_fb + 3296)
        fb_rel = place("fb_rel", [P, 1], F32, o_fb + 3328)
        zT_at = wbase + X * WSZ - 25024
        o = (o + 31) // 32 * 32
        gW1_sb = place("gW1_sb", [128, 2, HID], F32, o)
        assert wbase + 3 * WSZ + 4 * N * 4 <= o and o + 4096 <= zT_at
        zT = place("zT", [128, 2, N], F32, zT_at)
        cT = zT
        tT = place("tT", [128, 4, N], F32, wbase + 3 * WSZ)
        win = [place(f"win{i}", [HB, 2 * WIN], I32, zT_at + i * 3008) for i in range(2)]
        wq = [place(f"wq{i}", [HB, WIN], F32, zT_at + 6016 + i * 1504) for i in range(2)]
        wkey = [place(f"wkey{i}", [HB, WIN], F32, zT_at + 9024 + i * 1504) for i in range(2)]
        wlow = [place(f"wlow{i}", [HB, WIN], F32, zT_at + 12032 + i * 1504) for i in range(2)]
        dst_nat = place("dst_nat", [P, EROW], I32, work)
        dstf = place("dstf", [P, EROW], F32, work + 1728)
        over = place("over", [P, EROW], F16, work + 3456)
        last_cmp = place("last_cmp", [P, SEG, NB], F16, work + 4320)
        first_cmp = place("first_cmp", [P, SEG, NB], F16, work + 4320 + 6816)
        zs = [place(f"zs{i}", [P, D], F32, work + 18016 + 1024 * i) for i in range(2)]
        xagain = place("xagain", [P, XG * S, D], F32, work)
        o = wbase + 5 * WSZ
        y = place("y", [P, S, D], F32, o)
        rows = place("rows", [P, S, 2, ROW], F32, o + 5120)
        uS = [place(f"uS{i}", [128, 2, P], F32, o + 15424 + 1024 * i) for i in range(2)]
        yT = [place(f"yT{i}", [128, 2, P], F32, o + 17472 + 1024 * i) for i in range(2)]
        gW2_sb = place("gW2_sb", [128, 4, D], F32, wbase + 2 * WSZ + 8192)
        assert o + 19520 <= zT_at
        o = work
        xs = [place(f"xs{i}", [T, ROW], F32, o + 1056 * i) for i in range(4)]
        o += 4224
        xe = [place(f"xe{i}", [128, 2, T], F32, o + 1024 * i) for i in range(2)]
        o += 2048
        xp = [place(f"xp{i}", [128, 2, 2, T], F16, o + 1024 * i) for i in range(2)]
        o += 2048
        act = place("act", [128, 8, T], F32, o)
        o += 4096
        ap_ = [place(f"ap{i}", [128, 2, 8, T], F16, o + 4096 * i) for i in range(2)]
        o += 8192
        ys = [place(f"ys{i}", [T, D], F32, o + 1024 * i) for i in range(2)]
        o += 2048
        res = place("res", [P, 2, C, D], F32, wbase)

        window_rows = nc.dram_tensor("window_rows", [NWIN, 2 * WIN], I32).ap()
        h_table = nc.dram_tensor("h_table", [N, D], F32).ap()
        sorted_rows = nc.dram_tensor("sorted_rows", [X * CAP + SPARE * T, ROW], F32).ap()
        results = nc.dram_tensor("results", [2 * N + T, D], F32).ap()

        made = sem("constants_made")
        turned_made = sem("masks_made")
        dst_in = sem("dst_in")
        small_in = sem("vectors_in")
        late_in = sem("small_weights_in")
        gW2_in = sem("gW2_in")
        windows_out = sem("window_rows_written")
        vec = sem("vector_steps")
        cmp_ready = sem("segment_compares_ready")
        starts_summed = sem("starts_summed")
        starts_ready = sem("window_starts_ready")
        win_in = [sem(f"windows_in{i}") for i in range(2)]
        keys_made = sem("keys_made")
        keys_turned = sem("keys_turned")
        vecs_turned = sem("vectors_turned")
        flag_summed = sem("flag_summed")
        flag_ready = sem("flag_ready")
        x_in = [sem(f"x_in{i}") for i in range(G)]
        var_ready = sem("variances_ready")
        std_ready = sem("deviations_ready")
        norm_ready = sem("scales_ready")
        h_ready = sem("h_ready")
        parts_ready = sem("h_parts_ready")
        kc_ready = sem("chunk_keys_ready")
        onehots_ready = sem("onehots_ready")
        block_summed = sem("block_summed")
        counts_ready = sem("counts_ready")
        sums_ready = sem("sums_ready")
        z_ready = sem("z_ready")
        z_turned = sem("z_turned")
        zT_ready = sem("zT_ready")
        fb_in = sem("general_inputs_in")
        fb_zero = sem("general_sums_cleared")
        fb_index_ready = sem("general_index_ready")
        fb_gathered = sem("general_rows_in")
        fb_rel_ready = sem("general_place_ready")
        fb_hot_ready = sem("general_onehot_ready")
        fb_summed = sem("general_summed")
        fb_added = sem("general_added")
        fb_z = sem("general_z_ready")
        fb_turned = sem("general_z_turned")
        t_summed = sem("t_summed")
        t_ready = sem("t_ready")
        bn_var_ready = sem("batch_variance_ready")
        bn_std_ready = sem("batch_deviation_ready")
        bn_ready = sem("batch_scales_ready")
        t_normed = sem("t_normed")
        c_summed = sem("c_summed")
        c_ready = sem("c_ready")
        xagain_in = sem("x_again_in")
        u_ready = sem("u_ready")
        u_turned = sem("u_turned")
        x2_ready = sem("x2_ready")
        var2_ready = sem("row_variances_ready")
        std2_ready = sem("row_deviations_ready")
        norm2_ready = sem("row_scales_ready")
        y_ready = sem("y_ready")
        y_turned = sem("y_turned")
        yT_ready = sem("yT_ready")
        logits_summed = sem("logits_summed")
        both_ready = sem("choices_ready")
        slots_summed = sem("slots_summed")
        rows_ready = sem("rows_ready")
        rows_out = sem("rows_sent")
        pads_ready = sem("pads_ready")
        pads_out = sem("pads_sent")
        counted = sem("experts_counted")
        ends_summed = sem("ends_summed")
        tiles_ready = sem("tile_steps_ready")
        tiles_summed = sem("tile_steps_summed")
        table_ready = sem("tile_table_ready")
        mix_exp = sem("mix_exponentials_ready")
        stage_in = [sem(f"stage_in{i}") for i in range(3)]
        waited = sem("gpsimd_waited")
        fb_waited = sem("general_gpsimd_waited")
        w_scaled = sem("weight_scaled")
        hi_made = sem("weight_hi_made")
        weights_ready = sem("weights_ready")
        xs_in = [sem(f"xs_in{i}") for i in range(4)]
        xs_turned = sem("xs_turned")
        xe_ready = sem("xe_ready")
        xhi_ready = sem("xe_hi_ready")
        xp_ready = sem("xe_parts_ready")
        hid_summed = sem("hidden_summed")
        act_ready = sem("gelu_ready")
        ahi_ready = sem("gelu_hi_ready")
        ap_ready = sem("gelu_parts_ready")
        y_summed = sem("results_summed")
        ys_ready = sem("results_ready")
        scattered = sem("results_scattered")
        res_in = [sem(f"results_in{i}") for i in range(G)]
        mixed = sem("mixed")
        stored = sem("stored")

        block = ctx.enter_context(nc.Block())

        def load_rows(eng, to, of, done):
            eng.dma_start(to[0:112], of[0:112]).then_inc(done, 16)
            eng.dma_start(to[112:P], of[112:P]).then_inc(done, 16)

        def part_of(q):
            e, k = divmod(q, 4)
            if k < 2:
                return W1[e, 128 * k:128 * k + 128, :]
            return W2[e, 512 * (k - 2):512 * (k - 1), :].rearrange("(b p) d -> p b d", p=128)

        def stage_of(q):
            s = stage[q % 3][:, :]
            return s if q % 4 < 2 else s.rearrange("p (b d) -> p b d", d=D)

        def w_at(q, lo):
            e, k = divmod(q, 4)
            o = e * 8192 + (k // 2 * 2 + lo) * 2048 + k % 2 * 1024
            return wts[:, o:o + 1024]

        @block.sync
        def _(sp):
            dn = dst.rearrange("(p t) -> p t", p=P)
            x_t = x.rearrange("(c p) d -> p c d", p=P)
            load_rows(sp, dst_nat[:, :], dn, dst_in)
            sp.dma_start(next_dst[0:P - 1, :], dn[1:P, 0:1], allow_slow_non_contiguous=True).then_inc(dst_in, 16)
            for g in range(G):
                load_rows(sp, xraw[:, S * g:S * g + S, :], x_t[:, S * g:S * g + S, :], x_in[g])
            vectors = [(V_B1, X * 8, b1.rearrange("e (k p) -> (e k) p", p=128)),
                       (V_LNG, 2 * X, ln_g.rearrange("e (k p) -> (e k) p", p=128)),
                       (V_LNB, 2 * X, ln_b.rearrange("e (k p) -> (e k) p", p=128))]
            for to, of in ((V_GB1, gb1), (V_GG1, gg1), (V_GBT1, gbt1), (V_GB2, gb2), (V_GG2, gg2), (V_GBT2, gbt2)):
                r = of.rearrange("(k p) -> k p", p=128)
                vectors.append((to, r.shape[0], r))
            for to, n, of in vectors:
                sp.dma_start(vrows[to:to + n, :], of).then_inc(small_in, 16)
            sp.dma_start(eps1[:, :], bass.AP(eps_gin.tensor, 0, [[0, P], [1, 1]]), allow_slow_non_contiguous=True).then_inc(small_in, 16)
            sp.dma_start(gW1_sb[:, :, :], gW1.rearrange("(k p) n -> p k n", p=128)).then_inc(late_in, 16)
            sp.dma_start(Wr_sb[:, :, :], Wr.rearrange("(k p) n -> p k n", p=128)).then_inc(late_in, 16)
            sp.dma_start(br_sb[:, :], br.rearrange("(a n) -> a n", a=1)).then_inc(late_in, 16)
            sp.dma_start(b2_all[:, :, :], bass.AP(b2.tensor, 0, [[0, 128], [D, X], [1, D]])).then_inc(late_in, 16)

            def load_part(q):
                if q >= 3:
                    sp.wait_ge(weights_ready, q - 2)
                sp.dma_start(stage_of(q), part_of(q)).then_inc(stage_in[q % 3], 16)

            for q in range(3):
                load_part(q)
            sp.wait_ge(flag_ready, 1)
            verdict = sp.value_load(flag[0:1, 0:1], min_val=0, max_val=1 << 20)
            with sp.If(verdict == 0):
                sp.nop()
            with sp.Else():
                sp.wait_ge(h_ready, C)
                load_rows(sp, src_nat[:, :], src.rearrange("(p t) -> p t", p=P), fb_in)
                h_t = h_table.rearrange("(c p) d -> p c d", p=P)
                sp.dma_start(h_t[:, :, :], h32[:, :, :]).then_inc(fb_in, 16)
            for q in range(3, EARLY + 3):
                load_part(q)
            sp.wait_ge(pads_ready, 2)
            for k in range(SPARE):
                r = X * CAP + T * k
                sp.dma_start(sorted_rows[r:r + T, :], pad_row[:, :]).then_inc(pads_out, 16)
            sp.wait_ge(zT_ready, C)
            sp.dma_start(gW2_sb[:, :, :], gW2.rearrange("(k p) n -> p k n", p=128)).then_inc(gW2_in, 16)

            def load_again(g):
                o = S * (g % XG)
                load_rows(sp, xagain[:, o:o + S, :], x_t[:, S * g:S * g + S, :], xagain_in)

            for g in range(XG):
                load_again(g)
            for q in range(EARLY + 3, AFTER_CONV + 3):
                load_part(q)
            sp.wait_ge(x2_ready, S)
            load_again(XG)
            sp.wait_ge(table_ready, 3)
            for e in range(X):
                r = sp.value_load(pad_at[0:1, e:e + 1], min_val=0, max_val=X * CAP - T)
                sp.dma_start(sorted_rows[bass.ds(r, T), :], pad_row[:, :]).then_inc(pads_out, 16)
            sp.wait_ge(rows_out, 16 * 2 * C)
            sp.wait_ge(pads_out, 16 * (X + SPARE))

            def load_tile(i, b):
                r = sp.value_load(tile_row[0:1, bass.ds(i, 1)], min_val=0, max_val=X * CAP + (SPARE - 1) * T)
                sp.dma_start(xs[b][:, :], sorted_rows[bass.ds(r, T), :]).then_inc(xs_in[b], 16)

            for i in range(4):
                load_tile(i, i)
            for i in range(12):
                if i + AFTER_CONV + 3 < PARTS:
                    load_part(i + AFTER_CONV + 3)
                sp.wait_ge(scattered, 16 * (i + 1))
                load_tile(i + 4, i % 4)
            with sp.Fori(0, (NT - 1 - 12) // 4) as it:
                for k in range(4):
                    i = it * 4 + (12 + k)
                    sp.wait_ge(scattered, i * 16 + 16)
                    load_tile(i + 4, k)
            sp.wait_ge(scattered, 16 * NT)
            for k in range(4):
                sp.wait_ge(xs_in[k], 16 * (TAB // 4))
            r_t = results[0:2 * N, :].rearrange("(k c p) d -> p k c d", p=P, k=2)
            for g in range(G):
                for k in range(2):
                    load_rows(sp, res[:, k, S * g:S * g + S, :], r_t[:, k, S * g:S * g + S, :], res_in[g])
            o_t = out.rearrange("(c p) d -> p c d", p=P)
            for g in range(G):
                sp.wait_ge(mixed, 2 * S * (g + 1))
                load_rows(sp, o_t[:, S * g:S * g + S, :], x2[:, S * g:S * g + S, :], stored)
            sp.wait_ge(stored, 32 * G)

        @block.gpsimd
        def _(pool):
            g = nc.gpsimd
            g.memset(wait_src[:, :], 0.0).then_inc(made, 1)
            g.memset(ident[:, :], 0.0).then_inc(made, 1)
            g.memset(ones16[:, :], 1.0).then_inc(made, 1)
            g.memset(ones[:, :], 1.0).then_inc(made, 1)
            g.memset(before16[:, :], 1.0).then_inc(made, 1)
            g.memset(upto[:, :], 1.0).then_inc(made, 1)
            g.iota(node0[:, :], pattern=[[P, C + 1], [BW, BJ]], base=0, channel_multiplier=0,
                   allow_small_or_imprecise_dtypes=True).then_inc(made, 1)
            g.iota(key_iota[:, :], pattern=[[1, KEY]], base=0, channel_multiplier=0,
                   allow_small_or_imprecise_dtypes=True).then_inc(made, 1)
            pool.wait_ge(made, 8)
            g.affine_select(out=ident[:, :], in_=ident[:, :], compare_op=ALU.not_equal, fill=1.0, base=0,
                            pattern=[[-1, 128]], channel_multiplier=1).then_inc(turned_made, 1)
            for n, edges in enumerate((dst, src)):
                cols = window_rows[:, n * WIN:(n + 1) * WIN]
                for r0, r1 in ((0, NWIN // 16 * 16), (NWIN // 16 * 16, NWIN)):
                    of = bass.AP(edges.tensor, r0 * PITCH, [[PITCH, r1 - r0], [1, WIN]])
                    g.dma_start(cols[r0:r1, :], of).then_inc(windows_out, 16)
            g.affine_select(out=before16[:, :], in_=before16[:, :], compare_op=ALU.is_gt, fill=0.0, base=0,
                            pattern=[[1, P]], channel_multiplier=-1).then_inc(turned_made, 1)
            g.affine_select(out=upto[:, :], in_=upto[:, :], compare_op=ALU.is_ge, fill=0.0, base=0,
                            pattern=[[1, X]], channel_multiplier=-1).then_inc(turned_made, 1)
            g.iota(expert_iota[:, :], pattern=[[1, X]], base=0, channel_multiplier=0,
                   allow_small_or_imprecise_dtypes=True).then_inc(turned_made, 1)
            g.iota(expert_row[:, :], pattern=[[CAP, X]], base=0, channel_multiplier=0,
                   allow_small_or_imprecise_dtypes=True).then_inc(turned_made, 1)
            g.iota(token_id[:, :, :], pattern=[[N, 2], [P, C]], base=0, channel_multiplier=1)\
                .then_inc(turned_made, 1)
            g.iota(tile_no[:, :], pattern=[[1, TAB]], base=0, channel_multiplier=0,
                   allow_small_or_imprecise_dtypes=True).then_inc(turned_made, 1)
            g.memset(pad_row[:, :], 0.0).then_inc(pads_ready, 1)
            pool.wait_ge(pads_ready, 1)
            g.iota(pad_row[:, D:ROW].bitcast(I32), pattern=[[1, 1]], base=2 * N, channel_multiplier=1)\
                .then_inc(pads_ready, 1)
            pool.wait_ge(windows_out, 64)
            pool.wait_ge(starts_ready, 1)
            for i in range(2):
                g.indirect_dma_start(out=win[i][:, :], out_offset=None, in_=window_rows,
                                     in_offset=bass.IndirectOffsetOnAxis(ap=starti[:, i:i + 1], axis=0))\
                    .then_inc(win_in[i], 16)

            def carry_wait(done):
                g.tensor_tensor(after_wait[:, :], wait_src[:, :], wait_src[:, :], ALU.add).then_inc(done, 1)

            pool.wait_ge(flag_ready, 1)
            verdict = pool.value_load(flag[0:1, 0:1], min_val=0, max_val=1 << 20)
            with pool.If(verdict == 0):
                pool.nop()
            with pool.Else():
                pool.wait_ge(fb_in, 48)
                with pool.Fori(0, EROW) as t:
                    pool.wait_ge(fb_index_ready, t + 1)
                    carry_wait(fb_waited)
                    g.indirect_dma_start(out=gathered[:, :], out_offset=None, in_=h_table,
                                         in_offset=bass.IndirectOffsetOnAxis(ap=fb_index[:, 0:1], axis=0))\
                        .then_inc(fb_gathered, 16)
                    pool.wait_ge(fb_waited, t + 1)

            def split(q):
                s = stage[q % 3]
                pool.wait_ge(stage_in[q % 3], 16 * (q // 3 + 1))
                g.tensor_scalar(s[:, :], s[:, :], WSCALE, 1.0, ALU.mult, ALU.mult).then_inc(w_scaled, 1)
                pool.wait_ge(w_scaled, q + 1)
                g.tensor_scalar(w_at(q, 0), s[:, :], 1.0, 1.0, ALU.mult, ALU.mult).then_inc(hi_made, 1)
                pool.wait_ge(hi_made, q + 1)
                g.tensor_tensor(w_at(q, 1), s[:, :], w_at(q, 0), ALU.subtract).then_inc(weights_ready, 1)

            for q in range(EARLY):
                split(q)
            pool.wait_ge(zT_ready, C)
            for q in range(EARLY, AFTER_SUM):
                split(q)
            pool.wait_ge(c_summed, 14)
            for q in range(AFTER_SUM, AFTER_CONV):
                split(q)
            for c in range(C):
                s = c % S
                if s == 0:
                    pool.wait_ge(rows_ready, c // S + 1)
                for k in range(2):
                    g.indirect_dma_start(out=sorted_rows, out_offset=bass.IndirectOffsetOnAxis(
                        ap=sloti[:, k, s:s + 1], axis=0), in_=rows[:, s, k, :], in_offset=None)\
                        .then_inc(rows_out, 16)

            def scatter(i, b, r):
                if not isinstance(i, int) or i:
                    pool.wait_ge(scattered, i * 16)
                    pool.wait_ge(waited, i)
                pool.wait_ge(ys_ready, i + 1)
                carry_wait(waited)
                g.indirect_dma_start(out=results, out_offset=bass.IndirectOffsetOnAxis(
                    ap=xs[r][:, D:ROW].bitcast(I32), axis=0), in_=ys[b][:, :], in_offset=None)\
                    .then_inc(scattered, 16)

            pool.wait_ge(rows_out, 16 * 2 * C)
            for i in range(13):
                if i + AFTER_CONV < PARTS:
                    split(i + AFTER_CONV)
                scatter(i, i % 2, i % 4)
            with pool.Fori(0, (NT - 13) // 4) as it:
                for k in range(4):
                    i = it * 4 + (13 + k)
                    scatter(i, (13 + k) % 2, (13 + k) % 4)

        @block.vector
        def _(v):
            d = nc.vector
            vs = Steps(vec)

            def ordered():
                v.wait_ge(vec, vs.n)

            v.wait_ge(dst_in, 48)
            vs.inc(d.memset(bad[:, :], 0.0))
            vs.inc(d.tensor_copy(dstf[:, :], dst_nat[:, :]))
            ordered()
            vs.inc(d.tensor_tensor(over[:, 0:EROW - 1], dstf[:, 0:EROW - 1], dstf[:, 1:EROW], ALU.is_gt))
            vs.inc(d.tensor_tensor(bad[0:P - 1, 1:2], dstf[0:P - 1, EROW - 1:EROW], next_dst[0:P - 1, :],
                                   ALU.is_gt))
            ordered()
            v.wait_ge(made, 8)
            vs.inc(d.tensor_reduce(bad[:, 0:1], over[:, 0:EROW - 1], AX.X, ALU.add))
            seg = dstf[:, :].rearrange("p (k s) -> p k s", s=PITCH)
            first_node = node0[:, 0:NB].unsqueeze(1).to_broadcast([P, SEG, NB])
            next_node = node0[:, 1:NB + 1].unsqueeze(1).to_broadcast([P, SEG, NB])
            vs.inc(d.tensor_tensor(last_cmp[:, :, :], first_node,
                                   seg[:, :, PITCH - 1:PITCH].to_broadcast([P, SEG, NB]), ALU.is_gt))
            d.tensor_tensor(first_cmp[:, :, :], next_node, seg[:, :, 0:1].to_broadcast([P, SEG, NB]),
                            ALU.is_gt).then_inc(cmp_ready, 1)
            v.wait_ge(starts_summed, 1)
            vs.inc(d.tensor_copy(cnt[:, :], bank[0][0:HB, 0:6]))
            ordered()
            vs.inc(d.tensor_scalar_min(startf[:, :], cnt[:, 0:2], float(NWIN - 1)))
            ordered()
            d.tensor_copy(starti[:, :], startf[:, :]).then_inc(starts_ready, 1)
            vs.inc(d.tensor_tensor(missed[:, :], cnt[:, 2:4], startf[:, :], ALU.subtract))
            ordered()
            d.tensor_scalar(missed[:, :], missed[:, :], float(WIN // PITCH), None, ALU.is_gt)\
                .then_inc(starts_ready, 1)

            def parts(n):
                sl = slice(S * n, S * n + S)
                v.wait_ge(h_ready, S * n + S)
                vs.inc(d.tensor_copy(h16[:, sl, 0:D], h32[:, sl, :]))
                ordered()
                d.tensor_tensor(h16[:, sl, D:2 * D], h32[:, sl, :], h16[:, sl, 0:D], ALU.subtract)\
                    .then_inc(parts_ready, 1)

            def norm_group(n):
                b = n % 2
                v.wait_ge(x_in[n], 32)
                if n >= 2:
                    v.wait_ge(h_ready, S * (n - 1))
                first = vs.n
                for s in range(S):
                    vs.inc(d.bn_stats(stats[b][:, s, :], xraw[:, S * n + s, :]))
                for s in range(S):
                    v.wait_ge(vec, first + s + 1)
                    vs.inc(d.bn_aggr(mv[b][:, s, :], stats[b][:, s, :]))
                ordered()
                d.tensor_scalar_add(var_eps[b][:, :], mv[b][:, :, 1], EPS).then_inc(var_ready, 1)
                if n:
                    parts(n - 1)
                v.wait_ge(std_ready, n + 1)
                vs.inc(d.reciprocal(rstd[b][:, :], std[b][:, :]))
                ordered()
                d.scalar_tensor_tensor(out=shift[b][:, :], in0=mv[b][:, :, 0], scalar=-1.0, in1=rstd[b][:, :],
                                       op0=ALU.mult, op1=ALU.mult).then_inc(norm_ready, 1)

            def window_keys(i):
                v.wait_ge(win_in[i], 16)
                dcol, scol = win[i][:, 0:WIN], win[i][:, WIN:2 * WIN]
                vs.inc(d.tensor_scalar(wq[i][:, :], scol, -(P - 1) / 2.0, 1.0 / P, ALU.add, ALU.mult))
                vs.inc(d.tensor_scalar(wkey[i][:, :], dcol, cnt[:, 4 + i:5 + i], float(C), ALU.subtract, ALU.mult))
                ordered()
                vs.inc(d.tensor_scalar(wq[i][:, :], wq[i][:, :], MAGIC, MAGIC, ALU.add, ALU.subtract))
                ordered()
                vs.inc(d.scalar_tensor_tensor(out=wlow[i][:, :], in0=wq[i][:, :], scalar=-float(P), in1=scol,
                                              op0=ALU.mult, op1=ALU.add))
                d.tensor_tensor(wkey[i][:, :], wkey[i][:, :], wq[i][:, :], ALU.add).then_inc(keys_made, 1)

            norm_group(0)
            window_keys(0)
            window_keys(1)
            norm_group(1)
            v.wait_ge(keys_turned, 1)
            for i in range(2):
                for to, b in ((keys, 1 + i), (lows, 3 + i)):
                    vs.inc(d.tensor_copy(to[:, HB * i:HB * i + HB, :].rearrange("p b u -> p u b"),
                                         bank[b][0:P, 0:U * HB].rearrange("p (u b) -> p u b", u=U)))
            v.wait_ge(flag_summed, 1)
            d.tensor_copy(flag[:, :], bank[0][0:1, 8:9]).then_inc(flag_ready, 1)
            v.wait_ge(vecs_turned, 1)
            vs.inc(d.tensor_copy(vcols[:, :], bank[5][:, 0:NV]))
            v.wait_ge(small_in, 160)
            vs.inc(d.tensor_scalar_add(eps1[:, :], eps1[:, :], 1.0))
            for n in range(2, G):
                norm_group(n)
            parts(G - 1)

            def chunk(c, b):
                static = isinstance(c, int)
                if not static or c >= 2:
                    v.wait_ge(onehots_ready, c * BJ - BJ)
                d.tensor_copy(kc[b][:, 0, :, :], keys[:, bass.ds(c * BJ, BJ), :]).then_inc(kc_ready, 1)
                d.tensor_copy(kc[b][:, 1, :, :], lows[:, bass.ds(c * BJ, BJ), :]).then_inc(kc_ready, 1)
                v.wait_ge(kc_ready, c * 2 + 2)
                for j in range(BJ):
                    n = C * width(j)
                    if not static or c >= 1:
                        v.wait_ge(block_summed, c * BJ + (j + 1 - BJ))
                    for u in range(U):
                        d.tensor_scalar(key_hot[:, j, u, 0:n], key_iota[:, 0:n], kc[b][:, 0, j, u:u + 1],
                                        None, ALU.is_equal)
                        last = d.tensor_scalar(low_hot[:, j, u, :], key_iota[:, 0:P],
                                               kc[b][:, 1, j, u:u + 1], None, ALU.is_equal)
                    last.then_inc(onehots_ready, 1)
                    if j == 4 and (not static or c >= 2):
                        z(c - 2, b)

            def z(c, b):
                v.wait_ge(sums_ready, c + 1)
                if not isinstance(c, int) or c >= 2:
                    v.wait_ge(z_turned, c - 1)
                d.scalar_tensor_tensor(out=zs[b][:, :], in0=h32[:, bass.ds(c, 1), :].rearrange("p a d -> p (a d)"),
                                       scalar=eps1[:, 0:1], in1=bank[b][0:P, 0:D], op0=ALU.mult,
                                       op1=ALU.add).then_inc(z_ready, 1)

            v.wait_ge(flag_ready, 1)
            verdict = v.value_load(flag[0:1, 0:1], min_val=0, max_val=1 << 20)
            with v.If(verdict == 0):
                ordered()
                v.wait_ge(parts_ready, G)
                for c in range(3):
                    chunk(c, c % 2)
                with v.Fori(0, (C - 3) // 2) as i:
                    chunk(i * 2 + 3, 1)
                    chunk(i * 2 + 4, 0)
                z(C - 2, 1)
                z(C - 1, 0)
            with v.Else():
                ordered()
                v.wait_ge(fb_in, 48)
                v.wait_ge(parts_ready, G)
                d.memset(agg[:, :, :], 0.0).then_inc(fb_zero, 1)
                v.wait_ge(fb_zero, 1)
                with v.Fori(0, EROW) as t:
                    d.tensor_copy(fb_index[:, :], src_nat[:, bass.ds(t, 1)]).then_inc(fb_index_ready, 1)
                    v.wait_ge(fb_gathered, t * 16 + 16)
                    d.tensor_copy(fb_dst[:, :], dstf[:, bass.ds(t, 1)]).then_inc(fb_zero, 1)
                    with v.Fori(0, C) as c:
                        v.wait_ge(fb_zero, t + 2)
                        d.tensor_tensor(fb_rel[:, :], fb_dst[:, :], node0[:, bass.ds(c * BJ, 1)], ALU.subtract)\
                            .then_inc(fb_rel_ready, 1)
                        v.wait_ge(fb_rel_ready, t * C + c + 1)
                        d.tensor_scalar(fb_hot[:, :], key_iota[:, 0:P], fb_rel[:, 0:1], None, ALU.is_equal)\
                            .then_inc(fb_hot_ready, 1)
                        v.wait_ge(fb_summed, t * C + c + 1)
                        a = agg[:, bass.ds(c, 1), :].rearrange("p a d -> p (a d)")
                        d.tensor_tensor(a, bank[1][0:P, 0:D], a, ALU.add).then_inc(fb_added, 1)
                        v.wait_ge(fb_added, t * C + c + 1)
                with v.Fori(0, C) as c:
                    a = agg[:, bass.ds(c, 1), :].rearrange("p a d -> p (a d)")
                    hc = h32[:, bass.ds(c, 1), :].rearrange("p a d -> p (a d)")
                    d.scalar_tensor_tensor(out=zs[0][:, :], in0=hc, scalar=eps1[:, 0:1], in1=a,
                                           op0=ALU.mult, op1=ALU.add).then_inc(fb_z, 1)
                    v.wait_ge(fb_turned, c + 1)

            def batch_scales(m, bn, bt, gcol, btcol):
                one = slice(m, m + 1)
                ordered()
                vs.inc(d.bn_aggr(bn_mv[:, m, :], bn))
                ordered()
                d.tensor_scalar_add(bn_var[:, one], bn_mv[:, m, 1:2], EPS).then_inc(bn_var_ready, 1)
                v.wait_ge(bn_std_ready, m + 1)
                vs.inc(d.reciprocal(bn_r[:, one], bn_std[:, one]))
                ordered()
                vs.inc(d.tensor_tensor(bn_scale[:, one], bn_r[:, one], vcols[:, gcol:gcol + 1], ALU.mult))
                ordered()
                vs.inc(d.tensor_tensor(bn_ms[:, one], bn_mv[:, m, 0:1], bn_scale[:, one], ALU.mult))
                ordered()
                d.tensor_tensor(bn_shift[:, one], vcols[:, btcol:btcol + 1], bn_ms[:, one], ALU.subtract)\
                    .then_inc(bn_ready, 1)

            for m in range(4):
                for i, (c0, n) in enumerate(PIECES):
                    v.wait_ge(t_ready, 7 * m + i + 1)
                    vs.inc(d.bn_stats(bn1[:, m, i, :], tT[:, m, c0:c0 + n]))
                batch_scales(m, bn1[:, m, :, :].rearrange("p a b -> p (a b)"), None, V_GG1 + m, V_GBT1 + m)
            for i, (c0, n) in enumerate(PIECES):
                for f in range(2):
                    v.wait_ge(c_ready, 2 * i + f + 1)
                    vs.inc(d.bn_stats(bn2[:, f, i, :], cT[:, f, c0:c0 + n]))
            for f in range(2):
                batch_scales(4 + f, bn2[:, f, :, :].rearrange("p a b -> p (a b)"), None, V_GG2 + f, V_GBT2 + f)

            def add_x(n):
                for s in range(S):
                    c = S * n + s
                    v.wait_ge(u_turned, c + 1)
                    d.tensor_tensor(x2[:, c, :], bank[3 + c % 2][0:P, 0:D],
                                    xagain[:, c % (XG * S), :], ALU.add)\
                        .then_inc(x2_ready, 1)

            def row_stats(n, which, of, ready):
                first = vs.n
                for s in range(S):
                    ready(s)
                    vs.inc(d.bn_stats(stats[which][:, s, :], of(s)))
                for s in range(S):
                    v.wait_ge(vec, first + s + 1)
                    vs.inc(d.bn_aggr(mv[which][:, s, :], stats[which][:, s, :]))
                ordered()
                d.tensor_scalar_add(var_eps[which][:, :], mv[which][:, :, 1], EPS).then_inc(var2_ready, 1)

            def row_scales(n, which):
                v.wait_ge(std2_ready, 2 * n + which + 1)
                vs.inc(d.reciprocal(rstd[which][:, :], std[which][:, :]))
                ordered()
                d.scalar_tensor_tensor(out=shift[which][:, :], in0=mv[which][:, :, 0], scalar=-1.0,
                                       in1=rstd[which][:, :], op0=ALU.mult, op1=ALU.mult).then_inc(norm2_ready, 1)

            v.wait_ge(xagain_in, 32 * XG)
            vs.inc(d.memset(chosen[:, :], 0.0))
            add_x(0)
            for n in range(G):
                row_stats(n, 0, lambda s: x2[:, S * n + s, :], lambda s: v.wait_ge(x2_ready, S * n + s + 1))
                if n + 1 == XG:
                    v.wait_ge(xagain_in, 32 * G)
                if n + 1 < G:
                    add_x(n + 1)
                row_scales(n, 0)
                row_stats(n, 1, lambda s: y[:, s, :], lambda s: v.wait_ge(y_ready, S * n + s + 1))
                row_scales(n, 1)
                v.wait_ge(logits_summed, n + 1)
                vs.inc(d.tensor_copy(logits[:, :, :].rearrange("p s e -> p (s e)"), bank[0][0:P, 0:S * X]))
                ordered()
                first = vs.n
                for s in range(S):
                    vs.inc(d.max(best[:, s, :], logits[:, s, :]))
                for s in range(S):
                    v.wait_ge(vec, first + s + 1)
                    vs.inc(d.max_index(best_at[:, s, :], best[:, s, :], logits[:, s, :]))
                ordered()
                vs.inc(d.tensor_tensor(gap[:, S * n:S * n + S], best[:, :, 1], best[:, :, 0], ALU.subtract))
                vs.inc(d.tensor_copy(pick[:, :, :].rearrange("p k s -> p s k"), best_at[:, :, 0:2]))
                ordered()
                for k in range(2):
                    vs.inc(d.tensor_tensor(hot[:, k, :, :], pick[:, k, :].unsqueeze(2).to_broadcast([P, S, X]),
                                           expert_iota[:, :].unsqueeze(1).to_broadcast([P, S, X]), ALU.is_equal))
                ordered()
                d.tensor_tensor(both[:, :, :], hot[:, 0, :, :], hot[:, 1, :, :], ALU.add).then_inc(both_ready, 1)
                v.wait_ge(both_ready, n + 1)
                vs.inc(d.tensor_reduce(group_sum[:, :], both[:, :, :].rearrange("p s e -> p e s"), AX.X, ALU.add))
                if n:
                    v.wait_ge(rows_out, 16 * 2 * S * n)
                first = vs.n
                for s in range(S):
                    vs.inc(d.tensor_scalar(rows[:, s, 0, 0:D], y[:, s, :], rstd[1][:, s:s + 1],
                                           shift[1][:, s:s + 1], ALU.mult, ALU.add))
                ordered()
                vs.inc(d.tensor_copy(rows[:, :, 1, 0:D], rows[:, :, 0, 0:D]))
                for k in range(2):
                    vs.inc(d.tensor_copy(rows[:, :, k, D:ROW].bitcast(I32),
                                         token_id[:, k, S * n:S * n + S].unsqueeze(2)))
                v.wait_ge(slots_summed, n + 1)
                vs.inc(d.tensor_tensor(slot[:, :, :], bank[1][0:P, 0:S * X].rearrange("p (s e) -> p s e", e=X),
                                       expert_row[:, :].unsqueeze(1).to_broadcast([P, S, X]), ALU.add))
                ordered()
                vs.inc(d.tensor_tensor(chosen[:, :], chosen[:, :], group_sum[:, :], ALU.add))
                for k in range(2):
                    vs.inc(d.tensor_tensor(picked[:, k, :, :], slot[:, :, :], hot[:, k, :, :], ALU.mult))
                ordered()
                vs.inc(d.tensor_reduce(slotf[:, :, :], picked[:, :, :, :], AX.X, ALU.add))
                ordered()
                d.tensor_copy(sloti[:, :, :], slotf[:, :, :]).then_inc(rows_ready, 1)

            v.wait_ge(counted, 1)
            vs.inc(d.tensor_scalar(steps[:, 0:1], bank[2][0:X, 0:1], T / 2 - 0.5, 1.0 / T, ALU.add, ALU.mult))
            d.tensor_tensor(pad_at[0:1, :], bank[2][0:1, 8:8 + X], expert_row[0:1, :], ALU.add)\
                .then_inc(table_ready, 1)
            ordered()
            d.tensor_scalar(steps[:, 1:2], steps[:, 0:1], MAGIC, MAGIC, ALU.add, ALU.subtract)\
                .then_inc(tiles_ready, 1)
            v.wait_ge(tiles_ready, 1)
            vs.inc(d.tensor_scalar(steps[:, 2:3], steps[:, 1:2], -float(T), float(CAP), ALU.mult, ALU.add))
            v.wait_ge(ends_summed, 1)
            vs.inc(d.tensor_copy(steps[:, 3:4], bank[2][0:X, 16:17]))
            ordered()
            vs.inc(d.tensor_scalar(passed[:, 0, :], tile_no[:, :], steps[:, 3:4], steps[:, 2:3], ALU.is_ge, ALU.mult))
            d.tensor_scalar(passed[:, 1, :], tile_no[:, :], steps[:, 3:4], None, ALU.is_ge).then_inc(tiles_ready, 1)
            v.wait_ge(tiles_summed, 1)
            d.scalar_tensor_tensor(out=tile_row[:, :], in0=tile_no[0:1, :], scalar=float(T),
                                   in1=bank[2][0:1, 32:32 + TAB], op0=ALU.mult, op1=ALU.add).then_inc(table_ready, 1)
            d.tensor_scalar_min(tile_expert[:, :], bank[2][0:1, 128:128 + TAB], float(X - 1)).then_inc(table_ready, 1)
            v.wait_ge(mix_exp, 1)
            vs.inc(d.tensor_scalar_add(gap_sum[:, :], gap_exp[:, :], 1.0))
            ordered()
            vs.inc(d.reciprocal(mix[:, 0, :], gap_sum[:, :]))
            ordered()
            vs.inc(d.tensor_tensor(mix[:, 1, :], gap_exp[:, :], mix[:, 0, :], ALU.mult))

            v.wait_ge(table_ready, 3)

            def tile_input(i, b):
                e = v.value_load(tile_expert[0:1, bass.ds(i, 1)], min_val=0, max_val=X - 1)
                v.wait_ge(xs_turned, i + 1)
                if not isinstance(i, int) or i >= 2:
                    v.wait_ge(xp_ready, i - 1)
                for k in range(2):
                    ins = d.tensor_scalar(xe[b][:, k, :], bank[6 + b][:, T * k:T * k + T],
                                          vcols[:, bass.ds(e * 2 + (V_LNG + k), 1)],
                                          vcols[:, bass.ds(e * 2 + (V_LNB + k), 1)], ALU.mult, ALU.add)
                ins.then_inc(xe_ready, 1)
                v.wait_ge(xe_ready, i + 1)
                if not isinstance(i, int) or i >= 2:
                    v.wait_ge(hid_summed, i * 2 - 2)
                d.tensor_copy(xp[b][:, 0, :, :], xe[b][:, :, :]).then_inc(xhi_ready, 1)
                v.wait_ge(xhi_ready, i + 1)
                d.tensor_tensor(xp[b][:, 1, :, :], xe[b][:, :, :], xp[b][:, 0, :, :], ALU.subtract)\
                    .then_inc(xp_ready, 1)

            def tile_act(i, b, h):
                hb = slice(4 * h, 4 * h + 4)
                v.wait_ge(act_ready, i * 2 + (h + 1))
                if not isinstance(i, int) or i >= 2:
                    v.wait_ge(y_summed, i - 1)
                d.tensor_copy(ap_[b][:, 0, hb, :], act[:, hb, :]).then_inc(ahi_ready, 1)
                v.wait_ge(ahi_ready, i * 2 + (h + 1))
                d.tensor_tensor(ap_[b][:, 1, hb, :], act[:, hb, :], ap_[b][:, 0, hb, :], ALU.subtract)\
                    .then_inc(ap_ready, 1)

            def tile_result(i, b):
                e = v.value_load(tile_expert[0:1, bass.ds(i, 1)], min_val=0, max_val=X - 1)
                v.wait_ge(y_summed, i + 1)
                if not isinstance(i, int) or i >= 2:
                    v.wait_ge(scattered, i * 16 - 16)
                d.scalar_tensor_tensor(out=ys[b][:, :], in0=bank[4 + b][:, 0:D], scalar=1.0 / WSCALE,
                                       in1=b2_all[:, bass.ds(e, 1), :].rearrange("p a d -> p (a d)"),
                                       op0=ALU.mult, op1=ALU.add).then_inc(ys_ready, 1)

            tile_input(0, 0)
            tile_input(1, 1)
            tile_act(0, 0, 0)
            tile_act(0, 0, 1)

            def tile_step(i, b):
                tile_act(i + 1, 1 - b, 0)
                tile_input(i + 2, b)
                tile_act(i + 1, 1 - b, 1)
                tile_result(i, b)

            tile_step(0, 0)
            tile_step(1, 1)
            with v.Fori(0, (NT - 3) // 2) as it:
                for k in range(2):
                    tile_step(it * 2 + (2 + k), k)
            tile_result(NT - 1, 0)

            for g in range(G):
                v.wait_ge(res_in[g], 64)
                for k in range(2):
                    for s in range(S):
                        c = S * g + s
                        if k:
                            v.wait_ge(mixed, 2 * S * g + s + 1)
                        d.scalar_tensor_tensor(out=x2[:, c, :], in0=res[:, k, c, :], scalar=mix[:, k, c:c + 1],
                                               in1=x2[:, c, :], op0=ALU.mult, op1=ALU.add).then_inc(mixed, 1)

        @block.scalar
        def _(a):
            s_ = nc.scalar
            for n in range(G):
                b = n % 2
                a.wait_ge(var_ready, n + 1)
                s_.activation(std[b][:, :], var_eps[b][:, :], ACT.Sqrt).then_inc(std_ready, 1)
                a.wait_ge(norm_ready, n + 1)
                for s in range(S):
                    c = S * n + s
                    s_.activation(h32[:, c, :], xraw[:, c, :], ACT.Identity, scale=rstd[b][:, s:s + 1],
                                  bias=shift[b][:, s:s + 1]).then_inc(h_ready, 1)

            def chunk(c, b):
                static = isinstance(c, int)
                for j in range(BJ):
                    a.wait_ge(block_summed, c * BJ + (j + 1))
                    if j == 0 and (not static or c >= 2):
                        a.wait_ge(sums_ready, c - 1)
                    n = width(j)
                    s_.activation(counts[b][:, :, BW * j:BW * j + n],
                                  bank[5 + j % 2][0:P, 0:C * n].rearrange("p (n h) -> p h n", h=C),
                                  ACT.Copy).then_inc(counts_ready, 1)
                    if j == 7 and (not static or c >= 2):
                        store_zT(c - 2)

            def store_zT(c):
                a.wait_ge(z_turned, c + 1)
                s_.activation(zT[:, :, bass.ds(c * P, P)], bank[2][:, 0:2 * P].rearrange("p (k n) -> p k n", k=2),
                              ACT.Copy).then_inc(zT_ready, 1)

            a.wait_ge(flag_ready, 1)
            verdict = a.value_load(flag[0:1, 0:1], min_val=0, max_val=1 << 20)
            with a.If(verdict == 0):
                for c in range(3):
                    chunk(c, c % 2)
                with a.Fori(0, (C - 3) // 2) as i:
                    chunk(i * 2 + 3, 1)
                    chunk(i * 2 + 4, 0)
                store_zT(C - 2)
                store_zT(C - 1)
            with a.Else():
                with a.Fori(0, C) as c:
                    a.wait_ge(fb_turned, c + 1)
                    s_.activation(zT[:, :, bass.ds(c * P, P)],
                                  bank[2][:, 0:2 * P].rearrange("p (k n) -> p k n", k=2),
                                  ACT.Copy).then_inc(zT_ready, 1)

            def deviation(m):
                a.wait_ge(bn_var_ready, m + 1)
                s_.activation(bn_std[:, m:m + 1], bn_var[:, m:m + 1], ACT.Sqrt).then_inc(bn_std_ready, 1)

            for m in range(4):
                for i, (c0, n) in enumerate(PIECES):
                    q = 7 * m + i
                    a.wait_ge(t_summed, q + 1)
                    s_.activation(tT[:, m, c0:c0 + n], bank[3 + q % 4][:, 0:n], ACT.Identity,
                                  bias=vcols[:, V_GB1 + m:V_GB1 + m + 1]).then_inc(t_ready, 1)
                    if i == 1 and m:
                        deviation(m - 1)
                    if i == 3 and m:
                        a.wait_ge(bn_ready, m)
                        s_.activation(tT[:, m - 1, :], tT[:, m - 1, :], ACT.Relu, scale=bn_scale[:, m - 1:m],
                                      bias=bn_shift[:, m - 1:m]).then_inc(t_normed, 1)
            deviation(3)
            a.wait_ge(bn_ready, 4)

            def store_c(i):
                c0, n = PIECES[i]
                for f in range(2):
                    r = 2 * i + f
                    a.wait_ge(c_summed, r + 1)
                    s_.activation(cT[:, f, c0:c0 + n], bank[(0, 1, 2, 7)[r % 4]][:, 0:n], ACT.Identity,
                                  bias=vcols[:, V_GB2 + f:V_GB2 + f + 1]).then_inc(c_ready, 1)

            for i, (c0, n) in enumerate(PIECES):
                s_.activation(tT[:, 3, c0:c0 + n], tT[:, 3, c0:c0 + n], ACT.Relu, scale=bn_scale[:, 3:4],
                              bias=bn_shift[:, 3:4]).then_inc(t_normed, 1)
                if i:
                    store_c(i - 1)
            store_c(6)
            deviation(4)
            deviation(5)
            a.wait_ge(bn_ready, 6)

            def relu_tile(c):
                b = c % 2
                if c >= 2:
                    a.wait_ge(u_turned, c - 1)
                for f in range(2):
                    ins = s_.activation(uS[b][:, f, :], cT[:, f, P * c:P * c + P], ACT.Relu,
                                        scale=bn_scale[:, 4 + f:5 + f], bias=bn_shift[:, 4 + f:5 + f])
                ins.then_inc(u_ready, 1)

            for c in range(S):
                relu_tile(c)
            for n in range(G):
                a.wait_ge(var2_ready, 2 * n + 1)
                s_.activation(std[0][:, :], var_eps[0][:, :], ACT.Sqrt).then_inc(std2_ready, 1)
                if n + 1 < G:
                    for c in range(S * n + S, S * n + 2 * S):
                        relu_tile(c)
                a.wait_ge(norm2_ready, 2 * n + 1)
                for s in range(S):
                    c = S * n + s
                    if n:
                        a.wait_ge(rows_ready, n)
                        a.wait_ge(y_turned, S * n)
                    s_.activation(y[:, s, :], x2[:, c, :], ACT.Identity, scale=rstd[0][:, s:s + 1],
                                  bias=shift[0][:, s:s + 1]).then_inc(y_ready, 1)
                a.wait_ge(var2_ready, 2 * n + 2)
                s_.activation(std[1][:, :], var_eps[1][:, :], ACT.Sqrt).then_inc(std2_ready, 1)
                for s in range(S):
                    c = S * n + s
                    a.wait_ge(y_turned, c + 1)
                    s_.activation(yT[c % 2][:, :, :], bank[5 + c % 2][:, 0:2 * P].rearrange("p (k n) -> p k n", k=2),
                                  ACT.Copy).then_inc(yT_ready, 1)
            a.wait_ge(rows_ready, G)
            s_.activation(gap_exp[:, :], gap[:, :], ACT.Exp).then_inc(mix_exp, 1)

            a.wait_ge(table_ready, 3)

            def gelu(i, b):
                e = a.value_load(tile_expert[0:1, bass.ds(i, 1)], min_val=0, max_val=X - 1)
                for h in range(2):
                    a.wait_ge(hid_summed, i * 2 + (h + 1))
                    if not isinstance(i, int) or i >= 1:
                        a.wait_ge(ap_ready, i * 2 - 2 + (h + 1))
                    for q in range(4 * h, 4 * h + 4):
                        ins = s_.activation(act[:, q, :], bank[2 * b + h][:, T * (q % 4):T * (q % 4) + T],
                                            ACT.Gelu, scale=1.0 / WSCALE,
                                            bias=vcols[:, bass.ds(e * 8 + (V_B1 + q), 1)])
                    ins.then_inc(act_ready, 1)

            gelu(0, 0)
            with a.Fori(0, (NT - 1) // 4) as it:
                for k in range(4):
                    gelu(it * 4 + (k + 1), (k + 1) % 2)

        @block.tensor
        def _(pe):
            t = nc.tensor
            pe.wait_ge(made, 8)
            pe.wait_ge(turned_made, 1)
            pe.wait_ge(cmp_ready, 1)
            for i in range(2):
                hb = slice(HB * i, HB * i + HB)
                for col, of in ((i, last_cmp), (2 + i, first_cmp)):
                    for k in range(SEG):
                        t.matmul(bank[0][0:HB, col:col + 1], of[:, k, hb], ones16[0:P, 0:1],
                                 start=(k == 0), stop=(k == SEG - 1))
                last = t.matmul(bank[0][0:HB, 4 + i:5 + i], node0[0:1, hb], ones[0:1, 0:1], start=True, stop=True)
            last.then_inc(starts_summed, 1)
            pe.wait_ge(small_in, 160)
            t.transpose(bank[5][:, 0:NV], vrows[:, :], ident[0:NV, 0:NV]).then_inc(vecs_turned, 1)
            for i in range(2):
                pe.wait_ge(keys_made, i + 1)
                pe.wait_ge(vec, 1)
                for u in range(U):
                    t.transpose(bank[1 + i][0:P, HB * u:HB * u + HB], wkey[i][:, P * u:P * u + P], ident[0:HB, 0:HB])
                    last = t.transpose(bank[3 + i][0:P, HB * u:HB * u + HB], wlow[i][:, P * u:P * u + P],
                                       ident[0:HB, 0:HB])
            last.then_inc(keys_turned, 1)
            pe.wait_ge(starts_ready, 2)
            flags = ((bad[:, 0:1], P), (bad[:, 1:2], P), (missed[:, 0:1], HB), (missed[:, 1:2], HB))
            for n, (of, k) in enumerate(flags):
                last = t.matmul(bank[0][0:1, 8:9], of, ones[0:k, 0:1], start=(n == 0), stop=(n == 3))
            last.then_inc(flag_summed, 1)

            SHARE = [0, 3, 3, 4, 4, 4, 4, 3]

            def dense(c, b, k0, k1):
                for k in range(k0, k1):
                    for part in range(2):
                        last = t.matmul(bank[b][0:P, 0:D], counts[b][:, k, :], h16[:, k, D * part:D * part + D],
                                        start=(k == 0 and part == 0), stop=(k == C - 1 and part == 1))
                if k1 == C:
                    last.then_inc(sums_ready, 1)

            def turn_z(c, b):
                pe.wait_ge(z_ready, c + 1)
                if not isinstance(c, int) or c >= 1:
                    pe.wait_ge(zT_ready, c)
                for k in range(2):
                    last = t.transpose(bank[2][:, P * k:P * k + P], zs[b][:, 128 * k:128 * k + 128], ident[0:P, 0:P])
                last.then_inc(z_turned, 1)

            def chunk(c, b):
                static = isinstance(c, int)
                k0 = 0
                for j in range(BJ):
                    n = C * width(j)
                    pe.wait_ge(onehots_ready, c * BJ + (j + 1))
                    if not static or c or j >= 2:
                        pe.wait_ge(counts_ready, c * BJ + (j - 1))
                    for u in range(U):
                        last = t.matmul(bank[5 + j % 2][0:P, 0:n], low_hot[:, j, u, :], key_hot[:, j, u, 0:n],
                                        start=(u == 0), stop=(u == U - 1))
                    last.then_inc(block_summed, 1)
                    if static and c == 0:
                        continue
                    if j == 1:
                        pe.wait_ge(counts_ready, c * BJ)
                        if not static or c >= 3:
                            pe.wait_ge(z_ready, c - 2)
                    dense(c - 1, 1 - b, k0, k0 + SHARE[j])
                    k0 += SHARE[j]
                    if j == 6 and (not static or c >= 2):
                        turn_z(c - 2, b)

            pe.wait_ge(flag_ready, 1)
            verdict = pe.value_load(flag[0:1, 0:1], min_val=0, max_val=1 << 20)
            with pe.If(verdict == 0):
                pe.wait_ge(parts_ready, G)
                for c in range(3):
                    chunk(c, c % 2)
                with pe.Fori(0, (C - 3) // 2) as i:
                    chunk(i * 2 + 3, 1)
                    chunk(i * 2 + 4, 0)
                pe.wait_ge(counts_ready, C * BJ)
                pe.wait_ge(z_ready, C - 2)
                dense(C - 1, 0, 0, C)
                turn_z(C - 2, 1)
                turn_z(C - 1, 0)
            with pe.Else():
                with pe.Fori(0, EROW) as n:
                    with pe.Fori(0, C) as c:
                        pe.wait_ge(fb_hot_ready, n * C + c + 1)
                        t.matmul(bank[1][0:P, 0:D], fb_hot[:, :], gathered[:, :], start=True, stop=True)\
                            .then_inc(fb_summed, 1)
                with pe.Fori(0, C) as c:
                    pe.wait_ge(fb_z, c + 1)
                    for k in range(2):
                        last = t.transpose(bank[2][:, P * k:P * k + P], zs[0][:, 128 * k:128 * k + 128],
                                           ident[0:P, 0:P])
                    last.then_inc(fb_turned, 1)
                    pe.wait_ge(zT_ready, c + 1)

            pe.wait_ge(zT_ready, C)
            pe.wait_ge(late_in, 64)
            for m in range(4):
                for i, (c0, n) in enumerate(PIECES):
                    q = 7 * m + i
                    if q >= 4:
                        pe.wait_ge(t_ready, q - 3)
                    for k in range(2):
                        last = t.matmul(bank[3 + q % 4][:, 0:n], gW1_sb[:, k, 128 * m:128 * m + 128],
                                        zT[:, k, c0:c0 + n], start=(k == 0), stop=(k == 1))
                    last.then_inc(t_summed, 1)
            pe.wait_ge(gW2_in, 16)
            for i, (c0, n) in enumerate(PIECES):
                pe.wait_ge(t_normed, 3 + i + 1)
                for f in range(2):
                    r = 2 * i + f
                    to = bank[(0, 1, 2, 7)[r % 4]]
                    if r >= 4:
                        pe.wait_ge(c_ready, r - 3)
                    for k in range(4):
                        t.matmul(to[:, 0:n], gW2_sb[:, k, 128 * f:128 * f + 128], tT[:, k, c0:c0 + n],
                                 start=(k == 0), stop=False)
                    for s in range(n // P):
                        last = t.matmul(to[:, P * s:P * s + P], h32[:, c0 // P + s, 128 * f:128 * f + 128],
                                        ident[0:P, 0:P], start=False, stop=(s == n // P - 1))
                    last.then_inc(c_summed, 1)

            def turn_u(c):
                b = c % 2
                pe.wait_ge(u_ready, c + 1)
                if c >= 2:
                    pe.wait_ge(x2_ready, c - 1)
                for k in range(2):
                    last = t.transpose(bank[3 + b][0:P, 128 * k:128 * k + 128], uS[b][:, k, :], ident[:, :])
                last.then_inc(u_turned, 1)

            for c in range(S):
                turn_u(c)
            for n in range(G):
                if n + 1 < G:
                    for c in range(S * n + S, S * n + 2 * S):
                        turn_u(c)

                def turn_y(s):
                    c = S * n + s
                    pe.wait_ge(y_ready, c + 1)
                    if c >= 2:
                        pe.wait_ge(yT_ready, c - 1)
                    for k in range(2):
                        last = t.transpose(bank[5 + c % 2][:, P * k:P * k + P], y[:, s, 128 * k:128 * k + 128],
                                           ident[0:P, 0:P])
                    last.then_inc(y_turned, 1)

                turn_y(0)
                for s in range(S):
                    c = S * n + s
                    if s + 1 < S:
                        turn_y(s + 1)
                    pe.wait_ge(yT_ready, c + 1)
                    if n and s == 0:
                        pe.wait_ge(both_ready, n)
                    o = bank[0][0:P, X * s:X * s + X]
                    for k in range(2):
                        t.matmul(o, yT[c % 2][:, k, :], Wr_sb[:, k, :], start=(k == 0), stop=False)
                    last = t.matmul(o, ones[0:1, 0:P], br_sb[:, :], start=False, stop=True)
                last.then_inc(logits_summed, 1)
                pe.wait_ge(both_ready, n + 1)
                if n:
                    pe.wait_ge(rows_ready, n)
                for s in range(S):
                    o = bank[1][0:P, X * s:X * s + X]
                    t.matmul(o, before16[:, :], both[:, s, :], start=True, stop=False)
                    for s1 in range(s):
                        t.matmul(o, ones16[0:P, 0:P], both[:, s1, :], start=False, stop=False)
                    last = t.matmul(o, ones16[0:P, 0:P], chosen[:, :], start=False, stop=True)
                last.then_inc(slots_summed, 1)
            pe.wait_ge(rows_ready, G)
            t.matmul(bank[2][0:X, 0:1], chosen[:, :], ones16[0:P, 0:1], start=True, stop=True)
            t.matmul(bank[2][0:1, 8:8 + X], ones16[0:P, 0:1], chosen[:, :], start=True, stop=True)\
                .then_inc(counted, 1)
            pe.wait_ge(tiles_ready, 1)
            t.matmul(bank[2][0:X, 16:17], upto[:, :], steps[:, 1:2], start=True, stop=True).then_inc(ends_summed, 1)
            pe.wait_ge(tiles_ready, 2)
            for k in range(2):
                last = t.matmul(bank[2][0:1, 32 + 96 * k:32 + 96 * k + TAB], ones[0:X, 0:1], passed[:, k, :],
                                start=True, stop=True)
            last.then_inc(tiles_summed, 1)

            pe.wait_ge(table_ready, 3)

            def turn_rows(r, b, laps):
                pe.wait_ge(xs_in[r], laps * 16 + 16)
                for k in range(2):
                    last = t.transpose(bank[6 + b][:, T * k:T * k + T], xs[r][:, 128 * k:128 * k + 128], ident[:, :])
                last.then_inc(xs_turned, 1)

            def hidden(i, b):
                e = pe.value_load(tile_expert[0:1, bass.ds(i, 1)], min_val=0, max_val=X - 1)
                pe.wait_ge(weights_ready, e * 4 + 4)
                pe.wait_ge(xp_ready, i + 1)
                for h in range(2):
                    if not isinstance(i, int) or i >= 2:
                        pe.wait_ge(act_ready, i * 2 - 4 + (h + 1))
                    for q in range(4 * h, 4 * h + 4):
                        terms = [(wlo, xlo, k) for wlo, xlo in ((0, 0), (0, 1), (1, 0)) for k in range(2)]
                        for n, (wlo, xlo, k) in enumerate(terms):
                            last = t.matmul(bank[2 * b + h][:, T * (q % 4):T * (q % 4) + T],
                                            wts[:, bass.ds(e * 8192 + (wlo * 2048 + k * 1024 + 128 * q), 128)],
                                            xp[b][:, xlo, k, :], start=(n == 0), stop=(n == 5))
                    last.then_inc(hid_summed, 1)

            def result(i, b):
                e = pe.value_load(tile_expert[0:1, bass.ds(i, 1)], min_val=0, max_val=X - 1)
                if not isinstance(i, int) or i >= 2:
                    pe.wait_ge(ys_ready, i - 1)
                for h in range(2):
                    pe.wait_ge(ap_ready, i * 2 + (h + 1))
                    for q in range(4 * h, 4 * h + 4):
                        for n, (alo, wlo) in enumerate(((0, 0), (1, 0), (0, 1))):
                            last = t.matmul(bank[4 + b][:, 0:D], ap_[b][:, alo, q, :],
                                            wts[:, bass.ds(e * 8192 + ((2 + wlo) * 2048 + D * q), D)],
                                            start=(q == 0 and n == 0), stop=(q == 7 and n == 2))
                last.then_inc(y_summed, 1)

            turn_rows(0, 0, 0)
            turn_rows(1, 1, 0)
            hidden(0, 0)

            def tile_step(i, k, laps):
                hidden(i + 1, (k + 1) % 2)
                pe.wait_ge(xe_ready, i + 1)
                turn_rows((k + 2) % 4, k % 2, laps + (k + 2) // 4)
                result(i, k % 2)

            for k in range(4):
                tile_step(k, k, 0)
            with pe.Fori(0, (NT - 1) // 4 - 1) as it:
                for k in range(4):
                    tile_step(it * 4 + (4 + k), k, it + 1)
            result(NT - 1, 0)


_INS = ['x', 'src', 'dst', 'L0_gnn_W1', 'L0_gnn_b1', 'L0_gnn_g1', 'L0_gnn_bt1', 'L0_gnn_W2', 'L0_gnn_b2',
        'L0_gnn_g2', 'L0_gnn_bt2', 'L0_gnn_eps_gin', 'L0_ffn_Wr', 'L0_ffn_br', 'L0_ffn_ln_g', 'L0_ffn_ln_b',
        'L0_ffn_W1', 'L0_ffn_b1', 'L0_ffn_W2', 'L0_ffn_b2']


def kernel(**inputs):
    import numpy as _np
    import concourse.bacc as _bacc
    from concourse import mybir as _mybir
    from concourse.bass_utils import run_bass_kernel_spmd as _run

    nc = _bacc.Bacc("TRN2", target_bir_lowering=False, num_devices=1)
    arrays, args = {}, []
    for name in _INS:
        a = _np.ascontiguousarray(inputs[name])
        if a.ndim == 0:
            a = a.reshape(1)
        arrays[f"in_{name}_dram"] = a
        args.append(nc.dram_tensor(f"in_{name}_dram", a.shape, _mybir.dt.from_np(a.dtype), kind="ExternalInput").ap())
    args.append(nc.dram_tensor("out_0_dram", (N, D), _mybir.dt.float32, kind="ExternalOutput").ap())
    build(nc, *args)
    r = _run(nc, [arrays], core_ids=[0])
    return r.results[0]["out_0_dram"]
```
